# Optimizing a Trainium2 kernel written in Bass

```python
import numpy as np
import jax
import jax.numpy as jnp

def _softmax(x, axis=-1):
    return jax.nn.softmax(x, axis=axis)

def _gelu(x):
    return jax.nn.gelu(x, approximate=True)

def _silu(x):
    return jax.nn.silu(x)

def _sigmoid(x):
    return jax.nn.sigmoid(x)

def _layernorm(x, axis=-1, eps=1e-05):
    m = jnp.mean(x, axis=axis, keepdims=True)
    v = jnp.var(x, axis=axis, keepdims=True)
    return (x - m) / jnp.sqrt(v + eps)

def _scatter_add(tgt, idx, src, axis=0):
    return tgt.at[idx].add(src)

def _segment_sum(src, seg, n):
    return jax.ops.segment_sum(src, seg, n)
kernel_name = 'mk_cond_seq_d1_seqx_r4_e78fef'

def setup_inputs(seed: int=0):
    np.random.seed(seed)
    _w = jnp.asarray

    def _rec_inputs():
        import jax
        import jax.numpy as jnp
        _rk = jax.random.key(seed)
        x = -0.0002928 + 1 * jax.random.normal(jax.random.fold_in(_rk, 1), (32, 64, 256), jnp.float32)
        _lenS = 64 - jax.random.randint(jax.random.fold_in(_rk, 7), (32,), 0, max(1, 64 // 4) + 1, jnp.int32)
        _lenS2 = 64 - jax.random.randint(jax.random.fold_in(_rk, 8), (32,), 0, max(1, 64 // 4) + 1, jnp.int32)
        itok_B_0_7 = jax.random.randint(jax.random.fold_in(_rk, 11), (32,), 0, 8, jnp.int32)
        return (x, itok_B_0_7)
    x, itok_B_0_7 = _rec_inputs()

    def _L0_cond_setup():
        import jax, jax.numpy as jnp
        import numpy as np
        E, H, I = (8, 256, 1024)
        B, S = (4, 256)
        LN_EPS = 1e-12
        key = jax.random.key(seed)
        ks = jax.random.split(key, 8)
        x = jax.random.normal(ks[0], (B, S, H), dtype=jnp.float32)
        expert_idx = jax.random.randint(ks[1], (B,), 0, E, dtype=jnp.int64)
        Wi = jax.random.normal(ks[2], (E, H, I), dtype=jnp.float32) * 0.02
        bi = jnp.zeros((E, I), dtype=jnp.float32)
        Wo = jax.random.normal(ks[3], (E, I, H), dtype=jnp.float32) * 0.02
        bo = jnp.zeros((E, H), dtype=jnp.float32)
        gamma = jnp.ones((E, H), dtype=jnp.float32)
        beta = jnp.zeros((E, H), dtype=jnp.float32)
        return {'input_tensor': x, 'expert_idx': expert_idx, 'Wi': Wi, 'bi': bi, 'Wo': Wo, 'bo': bo, 'gamma': gamma, 'beta': beta}
    _L0_cond_all = _L0_cond_setup()
    _L0_cond_in = {k: v for k, v in _L0_cond_all.items() if k in ('Wi', 'bi', 'Wo', 'bo', 'gamma', 'beta')}
    del _L0_cond_all
    return {'x': x, 'itok_B_0_7': itok_B_0_7, 'L0_cond_Wi': _L0_cond_in['Wi'], 'L0_cond_bi': _L0_cond_in['bi'], 'L0_cond_Wo': _L0_cond_in['Wo'], 'L0_cond_bo': _L0_cond_in['bo'], 'L0_cond_gamma': _L0_cond_in['gamma'], 'L0_cond_beta': _L0_cond_in['beta']}

def reference(x, itok_B_0_7, L0_cond_Wi, L0_cond_bi, L0_cond_Wo, L0_cond_bo, L0_cond_gamma, L0_cond_beta):
    import jax
    import jax.numpy as jnp

    def _L0_cond_ref(input_tensor, expert_idx, Wi, bi, Wo, bo, gamma, beta):
        import jax, jax.numpy as jnp
        import numpy as np
        E, H, I = (8, 256, 1024)
        B, S = (4, 256)
        LN_EPS = 1e-12
        Wi_b = Wi[expert_idx]
        bi_b = bi[expert_idx]
        Wo_b = Wo[expert_idx]
        bo_b = bo[expert_idx]
        g_b = gamma[expert_idx]
        be_b = beta[expert_idx]
        h = jax.nn.gelu(jnp.einsum('bsh,bhi->bsi', input_tensor, Wi_b) + bi_b[:, None, :], approximate=False)
        o = jnp.einsum('bsi,bih->bsh', h, Wo_b) + bo_b[:, None, :]
        r = o + input_tensor
        mu = jnp.mean(r, axis=-1, keepdims=True)
        var = jnp.mean(jnp.square(r - mu), axis=-1, keepdims=True)
        y = (r - mu) * jax.lax.rsqrt(var + LN_EPS)
        return y * g_b[:, None, :] + be_b[:, None, :]
    x = _L0_cond_ref(x, itok_B_0_7, L0_cond_Wi, L0_cond_bi, L0_cond_Wo, L0_cond_bo, L0_cond_gamma, L0_cond_beta)
    return x

_drawn_inputs = setup_inputs


def setup_inputs(seed=0):
    import zlib

    import numpy as np

    out = dict(_drawn_inputs(seed))
    spreads = {'L0_cond_bi': (0.0, 0.1),
     'L0_cond_bo': (0.0, 0.1),
     'L0_cond_gamma': (1.0, 0.2),
     'L0_cond_beta': (0.0, 0.1)}
    factors = {}
    for name, (base, spread) in spreads.items():
        noise = np.random.default_rng([zlib.crc32(name.encode()), seed]).standard_normal(out[name].shape)
        drawn = base * np.exp(spread * noise) if base else spread * noise
        out[name] = jnp.asarray(drawn.astype(out[name].dtype))
    for name, factor in factors.items():
        out[name] = (out[name] * factor).astype(out[name].dtype)
    return out
```

```python
from contextlib import ExitStack

import concourse.bass as bass
from concourse import mybir

FP32 = mybir.dt.float32
I32 = mybir.dt.int32
ALU = mybir.AluOpType
ACT = mybir.ActivationFunctionType

P = 128
LN_EPS = 1e-12


def expert_ffn(nc, x, idx, Wi, bi, Wo, bo, gamma, beta, out):
    B, S, H = x.shape
    E, _, I = Wi.shape
    PAIR = P // S
    HC, IC = H // P, I // P
    MAX_BLOCKS = (B + E) // PAIR
    TILES = MAX_BLOCKS + 2
    SLOTS_X = TILES * PAIR
    LN_STEPS = 4
    assert PAIR == 2
    T_SRC, T_VALID, T_EXPERT, T_BEGIN, T_END = 0, SLOTS_X, 2 * SLOTS_X, 3 * SLOTS_X, 3 * SLOTS_X + E
    T_ALL = 3 * SLOTS_X + 2 * E

    ctx = ExitStack()
    with ctx:
        def sb(name, shape, dt=FP32):
            return ctx.enter_context(nc.sbuf_tensor(name, shape, dt))

        def pb(name, shape, dt=FP32):
            return ctx.enter_context(nc.psum_tensor(name, shape, dt))

        def sem(name):
            return ctx.enter_context(nc.semaphore(name))

        wi = sb("wi", [P, E, HC, I])
        wo = sb("wo", [P, E, IC, H])
        x_in = sb("x_in", [P, H])
        xs = sb("xs", [P, TILES + 1, H])
        xT = sb("xT", [P, 2, HC, P])
        h = sb("h", [P, IC, P])
        biT = sb("biT", [P, E * IC])
        bi_rows = sb("bi_rows", [E * IC, P])
        bo_bc = sb("bo_bc", [P, E, H])
        gamma_bc = sb("gamma_bc", [P, E, H])
        beta_bc = sb("beta_bc", [P, E, H])
        ident = sb("ident", [P, P])
        r = sb("r", [P, H])
        centred = sb("centred", [P, H])
        stats = sb("stats", [P, 6])
        meanvar = sb("meanvar", [P, 2])
        var_eps = sb("var_eps", [P, 1])
        minus_half = sb("minus_half", [P, 1])
        rstd = sb("rstd", [P, 1])
        idx_i = sb("idx_i", [B, 1], I32)
        idx_f = sb("idx_f", [B, 1])
        expert_iota = sb("expert_iota", [B, E])
        slot_iota = sb("slot_iota", [B, SLOTS_X])
        sample_iota = sb("sample_iota", [B, 1])
        before = sb("before", [B, B])
        ones = sb("ones", [B, B])
        onehot = sb("onehot", [B, E])
        pairs_i = sb("pairs_i", [B, E], I32)
        halved_i = sb("halved_i", [B, E], I32)
        nblocks = sb("nblocks", [B, E])
        ends = sb("ends", [B, 2 * E])
        place = sb("place", [B, E])
        placed = sb("placed", [B, E])
        slot_of = sb("slot_of", [B, 1])
        perm = sb("perm", [B, SLOTS_X])
        table = sb("table", [1, T_ALL], I32)

        preact = pb("preact", [P, IC // 2, 512])
        sums = pb("sums", [P, 512])[:, 0:H]
        xT_ps = pb("xT_ps", [P, 512])
        tab_ps = pb("tab_ps", [P, 512])

        def xs_row(n):
            return xs[:, bass.ds(n, 1), :].rearrange("p o h -> p (o h)")

        def preact_chunk(c):
            return preact[:, c // 2, (c % 2) * P:(c % 2 + 1) * P]

        idx_loaded = sem("idx_loaded")
        bi_loaded = sem("bi_loaded")
        rows_loaded = sem("rows_loaded")
        w_loaded = [sem(f"w_loaded{e}") for e in range(E)]
        x_loaded = sem("x_loaded")
        const_step = sem("const_step")
        sort_step = sem("sort_step")
        ranked = sem("ranked")
        permuted = sem("permuted")
        table_ready = sem("table_ready")
        biT_ps_ready = sem("biT_ps_ready")
        biT_ready = sem("biT_ready")
        xT_ps_ready = sem("xT_ps_ready")
        xT_ready = sem("xT_ready")
        preact_ready = sem("preact_ready")
        gelu_done = sem("gelu_done")
        h_used = sem("h_used")
        x_biased = sem("x_biased")
        sums_free = sem("sums_free")
        ln_step = sem("ln_step")
        var_ready = sem("var_ready")
        rstd_ready = sem("rstd_ready")
        y_ready = sem("y_ready")
        stored = sem("stored")

        block = ctx.enter_context(nc.Block())

        def load_weights(eng, e):
            eng.dma_start(wi[:, e, :, :], Wi[e, :, :].rearrange("(k p) n -> p k n", p=P)).then_inc(w_loaded[e], 16)
            eng.dma_start(wo[:, e, :, :], Wo[e, :, :].rearrange("(c p) n -> p c n", p=P)).then_inc(w_loaded[e], 16)

        def entry(eng, at, hi, lo=0):
            return eng.value_load(table[0:1, bass.ds(at, 1)], min_val=lo, max_val=hi)

        def all_blocks(eng):
            return entry(eng, T_END + E - 1, MAX_BLOCKS, B // PAIR)

        @block.sync
        def _(sp):
            sp.dma_start(idx_i[:, :], idx.rearrange("(b o) -> b o", o=1)).then_inc(idx_loaded, 16)
            sp.dma_start(bi_rows[:, :], bi.rearrange("e (c p) -> (e c) p", p=P)).then_inc(bi_loaded, 16)
            sp.wait_ge(table_ready, 1)


            def load_block(t):
                b0 = entry(sp, PAIR * t, B - 1)
                b1 = entry(sp, PAIR * t + 1, B - 1)
                if not isinstance(t, int) or t > 0:
                    sp.wait_ge(x_biased, t)
                for half, b in enumerate((b0, b1)):
                    sp.dma_start(x_in[half * S:(half + 1) * S, :],
                                 x[bass.ds(b, 1), :, :].rearrange("o s h -> (o s) h")).then_inc(x_loaded, 16)

            load_block(0)
            load_block(1)
            for e in range(E):
                if e + 1 < E:
                    load_weights(sp, e + 1)
                begin = entry(sp, T_BEGIN + e, MAX_BLOCKS)
                end = entry(sp, T_END + e, MAX_BLOCKS)
                with sp.If(begin < end):
                    with sp.Fori(begin + 2, end + 2) as t:
                        load_block(t)
                    sp.nop()
                with sp.Else():
                    sp.nop()

        @block.gpsimd
        def _(pool):
            nc.gpsimd.iota(expert_iota[:, :], [[1, E]], base=0, channel_multiplier=0,
                           allow_small_or_imprecise_dtypes=True).then_inc(const_step, 1)
            nc.gpsimd.iota(slot_iota[:, :], [[1, SLOTS_X]], base=0, channel_multiplier=0,
                           allow_small_or_imprecise_dtypes=True).then_inc(const_step, 1)
            nc.gpsimd.iota(sample_iota[:, :], [[0, 1]], base=0, channel_multiplier=1,
                           allow_small_or_imprecise_dtypes=True).then_inc(const_step, 1)
            nc.gpsimd.memset(ones[:, :], 1.0).then_inc(const_step, 1)
            nc.gpsimd.memset(ident[:, :], 0.0).then_inc(const_step, 1)
            nc.gpsimd.memset(minus_half[:, :], -0.5).then_inc(const_step, 1)
            pool.wait_ge(const_step, 6)
            nc.gpsimd.affine_select(out=before[:, :], in_=ones[:, :], compare_op=ALU.is_gt, fill=0.0, base=0,
                                    pattern=[[1, B]], channel_multiplier=-1).then_inc(const_step, 1)
            nc.gpsimd.affine_select(out=ident[:, :], in_=ident[:, :], compare_op=ALU.not_equal, fill=1.0, base=0,
                                    pattern=[[-1, P]], channel_multiplier=1).then_inc(const_step, 1)

            pool.wait_ge(table_ready, 1)
            blocks = all_blocks(pool)
            with pool.Fori(0, blocks) as j:
                pool.wait_ge(var_ready, j + 1)
                nc.gpsimd.tensor_tensor(rstd[:, :], var_eps[:, :], minus_half[:, :], ALU.pow).then_inc(rstd_ready, 1)
                pool.wait_ge(y_ready, j + 1)
                b0 = entry(pool, j * PAIR, B - 1)
                pool.dma_start(out[bass.ds(b0, 1), :, :].rearrange("o s h -> (o s) h"),
                               xs_row(j + 1)[0:S, :]).then_inc(stored, 16)
                b1 = entry(pool, j * PAIR + 1, B - 1)
                valid = entry(pool, j * PAIR + (T_VALID + 1), 1)
                with pool.If(valid > 0):
                    pool.dma_start(out[bass.ds(b1, 1), :, :].rearrange("o s h -> (o s) h"),
                                   xs_row(j + 1)[S:P, :]).then_inc(stored, 16)
                with pool.Else():
                    pool.nop()
            pool.wait_ge(stored, 16 * B)

        @block.scalar
        def _(act):
            load_weights(act, 0)
            for dst, src in ((bo_bc, bo), (gamma_bc, gamma), (beta_bc, beta)):
                act.dma_start(dst[:, :, :].rearrange("p e h -> p (e h)"),
                              src.rearrange("e h -> (e h)").partition_broadcast(P)).then_inc(rows_loaded, 16)
            act.sem_inc(gelu_done, IC)
            act.sem_inc(h_used, IC)
            act.wait_ge(table_ready, 1)
            act.wait_ge(biT_ready, 1)
            blocks = all_blocks(act)
            with act.Fori(0, blocks) as j:
                e = entry(act, j * PAIR + T_EXPERT, E - 1)
                for c in range(IC):
                    if c % 2 == 0:
                        act.wait_ge(preact_ready, j * IC + (c + 2))
                    act.wait_ge(h_used, j * IC + (c + 1))
                    nc.scalar.activation(h[:, c, :], preact_chunk(c), ACT.Gelu,
                                         bias=biT[:, bass.ds(e * IC + c, 1)]).then_inc(gelu_done, 1)

        @block.vector
        def _(dve):
            steps = [0]

            def chain(ins):
                steps[0] += 1
                ins.then_inc(sort_step, 1)
                dve.wait_ge(sort_step, steps[0])

            dve.wait_ge(idx_loaded, 16)
            dve.wait_ge(const_step, 8)
            chain(nc.vector.tensor_copy(idx_f[:, :], idx_i[:, :]))
            chain(nc.vector.tensor_scalar(onehot[:, :], expert_iota[:, :], idx_f[:, 0:1], None, ALU.is_equal))
            dve.wait_ge(ranked, 1)
            chain(nc.vector.tensor_scalar(pairs_i[:, :], tab_ps[0:B, E:2 * E], float(PAIR - 1), None, ALU.add))
            chain(nc.vector.tensor_scalar(halved_i[:, :], pairs_i[:, :], 1, None, ALU.logical_shift_right))
            chain(nc.vector.tensor_copy(nblocks[:, :], halved_i[:, :]))
            chain(nc.vector.tensor_tensor_scan(ends[:, E:2 * E], ones[:, 0:E], nblocks[:, :], 0.0, ALU.mult, ALU.add))
            chain(nc.vector.tensor_tensor(ends[:, 0:E], ends[:, E:2 * E], nblocks[:, :], ALU.subtract))
            chain(nc.vector.scalar_tensor_tensor(place[:, :], ends[:, 0:E], float(PAIR), tab_ps[0:B, 0:E],
                                                 ALU.mult, ALU.add))
            chain(nc.vector.tensor_tensor(placed[:, :], place[:, :], onehot[:, :], ALU.mult))
            chain(nc.vector.reduce_sum(slot_of[:, :], placed[:, :], mybir.AxisListType.X))
            chain(nc.vector.tensor_scalar(perm[:, :], slot_iota[:, :], slot_of[:, 0:1], None, ALU.is_equal))
            dve.wait_ge(permuted, 1)
            chain(nc.vector.tensor_copy(table[0:1, T_BEGIN:T_ALL], ends[0:1, :]))
            nc.vector.tensor_copy(table[0:1, 0:T_BEGIN], tab_ps[0:1, 2 * E:2 * E + 3 * SLOTS_X]).then_inc(table_ready, 1)
            dve.wait_ge(table_ready, 1)
            dve.wait_ge(biT_ps_ready, 1)
            nc.vector.tensor_copy(biT[:, :], tab_ps[:, 256:256 + E * IC]).then_inc(biT_ready, 1)

            def take_xT(t):
                dve.wait_ge(xT_ps_ready, t + 1)
                nc.vector.tensor_copy(xT[:, bass.ds(t % 2, 1), :, :].rearrange("p o k n -> p (o k n)"),
                                      xT_ps[:, 0:H]).then_inc(xT_ready, 1)
                e = entry(dve, t * PAIR + T_EXPERT, E - 1)
                nc.vector.tensor_tensor(xs_row(t + 1), x_in[:, :], bo_bc[:, bass.ds(e, 1), :].rearrange("p o h -> p (o h)"),
                                        ALU.add).then_inc(x_biased, 1)

            def layer_norm(n):
                e = entry(dve, n * PAIR + (T_EXPERT - PAIR), E - 1)
                dve.wait_ge(x_biased, n)
                dve.wait_ge(h_used, n * IC + IC)
                row = xs_row(n)
                nc.vector.tensor_tensor(r[:, :], sums, row, ALU.add).then_inc(sums_free, 1)
                dve.wait_ge(sums_free, n + 1)
                nc.vector.bn_stats(stats[:, :], r[:, :]).then_inc(ln_step, 1)
                dve.wait_ge(ln_step, n * LN_STEPS + 1)
                dve.sem_inc(ln_step, 1)
                nc.vector.bn_aggr(meanvar[:, :], stats[:, :]).then_inc(ln_step, 1)
                dve.wait_ge(ln_step, n * LN_STEPS + 3)
                nc.vector.tensor_scalar(var_eps[:, :], meanvar[:, 1:2], LN_EPS, None, ALU.add).then_inc(var_ready, 1)
                nc.vector.scalar_tensor_tensor(centred[:, :], r[:, :], meanvar[:, 0:1],
                                               gamma_bc[:, bass.ds(e, 1), :].rearrange("p o h -> p (o h)"),
                                               ALU.subtract, ALU.mult).then_inc(ln_step, 1)
                dve.wait_ge(ln_step, n * LN_STEPS + 4)
                dve.wait_ge(rstd_ready, n)
                nc.vector.scalar_tensor_tensor(row, centred[:, :], rstd[:, 0:1],
                                               beta_bc[:, bass.ds(e, 1), :].rearrange("p o h -> p (o h)"),
                                               ALU.mult, ALU.add).then_inc(y_ready, 1)

            dve.sem_inc(sums_free, 1)
            dve.sem_inc(ln_step, LN_STEPS)
            dve.wait_ge(rows_loaded, 16 * 3)
            blocks = all_blocks(dve)
            take_xT(0)
            take_xT(1)
            with dve.Fori(0, blocks) as j:
                take_xT(j + 2)
                with dve.If(j > 0):
                    layer_norm(j)
                with dve.Else():
                    dve.nop()
            layer_norm(blocks)

        @block.tensor
        def _(pe):
            pe.wait_ge(const_step, 8)
            pe.wait_ge(sort_step, 2)
            nc.tensor.matmul(tab_ps[0:B, 0:E], before[:, :], onehot[:, :], start=True, stop=True)
            nc.tensor.matmul(tab_ps[0:B, E:2 * E], ones[:, :], onehot[:, :], start=True, stop=True).then_inc(ranked, 1)
            pe.wait_ge(sort_step, 11)
            for n, column in enumerate((sample_iota, ones, idx_f)):
                at = 2 * E + n * SLOTS_X
                last = nc.tensor.matmul(tab_ps[0:1, at:at + SLOTS_X], column[:, 0:1], perm[:, :], start=True, stop=True)
            last.then_inc(permuted, 1)
            pe.wait_ge(bi_loaded, 16)
            pe.wait_ge(table_ready, 1)
            nc.tensor.transpose(tab_ps[:, 256:256 + E * IC], bi_rows[:, :],
                                ident[0:E * IC, 0:E * IC]).then_inc(biT_ps_ready, 1)

            def transpose_x(t):
                pe.wait_ge(x_loaded, t * (16 * PAIR) + 16 * PAIR)
                if not isinstance(t, int) or t > 0:
                    pe.wait_ge(xT_ready, t)
                for k in range(HC):
                    last = nc.tensor.transpose(xT_ps[:, k * P:(k + 1) * P],
                                               x_in[:, k * P:(k + 1) * P], ident[:, :])
                last.then_inc(xT_ps_ready, 1)

            def first_product(j, e):
                pe.wait_ge(xT_ready, j + 1)
                for c in range(IC):
                    if c % 2 == 0:
                        pe.wait_ge(gelu_done, j * IC + (c + 2))
                    for k in range(HC):
                        last = nc.tensor.matmul(preact_chunk(c), wi[:, e, k, c * P:(c + 1) * P],
                                                xT[:, bass.ds(j % 2, 1), k, :].rearrange("p o n -> p (o n)"),
                                                start=(k == 0), stop=(k == HC - 1))
                    last.then_inc(preact_ready, 1)

            def second_product(n):
                pe.wait_ge(sums_free, n)
                e = entry(pe, n * PAIR + (T_EXPERT - PAIR), E - 1)
                for c in range(IC):
                    pe.wait_ge(gelu_done, n * IC + (c + 1))
                    nc.tensor.matmul(sums, h[:, c, :],
                                     wo[:, bass.ds(e, 1), c, :].rearrange("p o n -> p (o n)"),
                                     start=(c == 0), stop=(c == IC - 1)).then_inc(h_used, 1)

            transpose_x(0)
            transpose_x(1)
            for e in range(E):
                begin = entry(pe, T_BEGIN + e, MAX_BLOCKS)
                end = entry(pe, T_END + e, MAX_BLOCKS)
                with pe.If(begin < end):
                    pe.wait_ge(w_loaded[e], 32)
                    with pe.Fori(begin, end) as j:
                        first_product(j, e)
                        transpose_x(j + 2)
                        with pe.If(j > 0):
                            second_product(j)
                        with pe.Else():
                            pe.nop()
                    pe.nop()
                with pe.Else():
                    pe.nop()
            second_product(all_blocks(pe))


INPUTS = ["x", "itok_B_0_7", "L0_cond_Wi", "L0_cond_bi", "L0_cond_Wo", "L0_cond_bo", "L0_cond_gamma", "L0_cond_beta"]


def kernel(**inputs):
    import numpy as np
    import concourse.bacc as bacc
    from concourse.bass_utils import run_bass_kernel_spmd

    nc = bacc.Bacc("TRN2", target_bir_lowering=False, num_devices=1)
    arrays, args = {}, []
    for name in INPUTS:
        a = np.ascontiguousarray(inputs[name])
        arrays[name + "_dram"] = a
        args.append(nc.dram_tensor(name + "_dram", a.shape, mybir.dt.from_np(a.dtype), kind="ExternalInput").ap())
    y = nc.dram_tensor("y_dram", inputs["x"].shape, FP32, kind="ExternalOutput").ap()
    expert_ffn(nc, *args, y)
    result = run_bass_kernel_spmd(nc, [arrays], core_ids=[0])
    return result.results[0]["y_dram"]
```

```python
from contextlib import ExitStack

import concourse.bass as bass
from concourse import mybir

FP32 = mybir.dt.float32
FP32R = mybir.dt.float32r
I32 = mybir.dt.int32
ALU = mybir.AluOpType
ACT = mybir.ActivationFunctionType

P = 128
LN_EPS = 1e-12


def expert_ffn(nc, x, idx, Wi, bi, Wo, bo, gamma, beta, out):
    B, S, H = x.shape
    E, _, I = Wi.shape
    PAIR = P // S
    HC, IC = H // P, I // P
    MAX_BLOCKS = (B + E) // PAIR
    TILES = MAX_BLOCKS + 2
    SLOTS_X = TILES * PAIR
    PEELED = 4
    OWN = 2
    PIECES = 4
    PER = IC // PIECES
    STORE_LAG = 6
    WARM_UP = 12
    LN_STEPS = 4
    assert PAIR == 2
    T_BEGIN, T_END, T_WORD = 0, E, 2 * E
    SECOND = B
    VALID = B * B
    EXPERT = 2 * VALID
    T_ALL = T_WORD + TILES

    ctx = ExitStack()
    with ctx:
        def sb(name, shape, dt=FP32):
            return ctx.enter_context(nc.sbuf_tensor(name, shape, dt))

        def pb(name, shape, dt=FP32):
            return ctx.enter_context(nc.psum_tensor(name, shape, dt))

        def sem(name):
            return ctx.enter_context(nc.semaphore(name))

        wi = sb("wi", [P, E, HC, I])
        wo_in = sb("wo_in", [P, 2, IC, H])
        wo_hi = sb("wo_hi", [P, 2, IC, H], FP32R)
        wo_lo = sb("wo_lo", [P, 2, IC, H], FP32R)
        x_in = sb("x_in", [P, 2 + OWN, H])
        xs = sb("xs", [P, TILES + 1, H])
        xT = sb("xT", [P, 2, HC, P])
        h = sb("h", [P, IC, P])
        h_hi = sb("h_hi", [P, IC, P], FP32R)
        h_lo = sb("h_lo", [P, IC, P], FP32R)
        biT = sb("biT", [P, E * IC])
        bi_rows = sb("bi_rows", [E * IC, P])
        bo_bc = sb("bo_bc", [P, E, H])
        gamma_bc = sb("gamma_bc", [P, E, H])
        beta_bc = sb("beta_bc", [P, E, H])
        ident = sb("ident", [P, P])
        r = sb("r", [P, H])
        centred = sb("centred", [P, H])
        stats = sb("stats", [P, 6])
        meanvar = sb("meanvar", [P, 2])
        var_eps = sb("var_eps", [P, 1])
        minus_half = sb("minus_half", [P, 1])
        rstd = sb("rstd", [P, 1])
        scratch = sb("scratch", [P, 1])
        idx_i = sb("idx_i", [B, 1], I32)
        idx_f = sb("idx_f", [B, 1])
        expert_iota = sb("expert_iota", [B, E])
        slot_iota = sb("slot_iota", [B, SLOTS_X])
        sample_iota = sb("sample_iota", [B, 1])
        before = sb("before", [B, B])
        ones = sb("ones", [B, B])
        onehot = sb("onehot", [B, E])
        pairs_i = sb("pairs_i", [B, E], I32)
        halved_i = sb("halved_i", [B, E], I32)
        nblocks = sb("nblocks", [B, E])
        ends = sb("ends", [B, 2 * E])
        place = sb("place", [B, E])
        placed = sb("placed", [B, E])
        slot_of = sb("slot_of", [B, 1])
        code = sb("code", [B, PAIR])
        perm = sb("perm", [B, SLOTS_X])
        table = sb("table", [1, T_ALL], I32)

        preact = pb("preact", [P, IC // 2, 512])
        sums_ps = pb("sums_ps", [P, 2, 512])
        xT_ps = pb("xT_ps", [P, 512])
        tab_ps = pb("tab_ps", [P, 512])

        def xs_row(n):
            return xs[:, bass.ds(n, 1), :].rearrange("p o h -> p (o h)")

        def sums(n):
            return sums_ps[:, bass.ds(n % 2, 1), 0:H].rearrange("p o h -> p (o h)")

        def preact_chunk(c):
            return preact[:, c // 2, (c % 2) * P:(c % 2 + 1) * P]

        idx_loaded = sem("idx_loaded")
        bi_loaded = sem("bi_loaded")
        bo_loaded = sem("bo_loaded")
        rows_loaded = [sem(f"rows_loaded{e}") for e in range(0, E, 2)]
        wi_loaded = [sem(f"wi_loaded{e}") for e in range(E)]
        wo_loaded = [sem(f"wo_loaded{s}") for s in range(2)]
        wo_hi_done = sem("wo_hi_done")
        wo_lo_done = sem("wo_lo_done")
        first_x_loaded = [sem(f"first_x_loaded{t}") for t in range(OWN)]
        x_loaded = sem("x_loaded")
        const_step = sem("const_step")
        sort_step = sem("sort_step")
        ranked = sem("ranked")
        permuted = sem("permuted")
        table_ready = sem("table_ready")
        biT_ps_ready = sem("biT_ps_ready")
        biT_ready = sem("biT_ready")
        xT_ps_ready = sem("xT_ps_ready")
        xT_ready = sem("xT_ready")
        preact_ready = sem("preact_ready")
        gelu_done = sem("gelu_done")
        h_hi_done = sem("h_hi_done")
        h_lo_done = sem("h_lo_done")
        h_used = sem("h_used")
        x_biased = sem("x_biased")
        sums_free = sem("sums_free")
        ln_step = sem("ln_step")
        var_ready = sem("var_ready")
        rstd_ready = sem("rstd_ready")
        y_ready = sem("y_ready")
        stored = sem("stored")

        block = ctx.enter_context(nc.Block())

        def load_wi(eng, e):
            eng.dma_start(wi[:, e, :, :], Wi[e, :, :].rearrange("(k p) n -> p k n", p=P)).then_inc(wi_loaded[e], 16)

        def load_wo(eng, e):
            if e >= 2:
                eng.wait_ge(wo_lo_done, e - 1)
            eng.dma_start(wo_in[:, e % 2, :, :], Wo[e, :, :].rearrange("(c p) n -> p c n", p=P)).then_inc(wo_loaded[e % 2], 16)

        def load_rows(eng, dst, src, e0, e1, done):
            eng.dma_start(dst[:, e0:e1, :].rearrange("p e h -> p (e h)"),
                          src[e0:e1, :].rearrange("e h -> (e h)").partition_broadcast(P)).then_inc(done, 16)

        def load_gamma_beta(eng, e):
            load_rows(eng, gamma_bc, gamma, e, e + 2, rows_loaded[e // 2])
            load_rows(eng, beta_bc, beta, e, e + 2, rows_loaded[e // 2])

        def own(t):
            return isinstance(t, int) and t < OWN

        def x_buffer(t):
            return 2 + t if own(t) else t % 2

        def x_rows(t):
            if isinstance(t, int):
                return x_in[:, x_buffer(t), :]
            return x_in[:, bass.ds(x_buffer(t), 1), :].rearrange("p o h -> p (o h)")

        def load_block(eng, k, halves=range(PAIR)):
            t = k + 1
            w = word(eng, t)
            if not isinstance(k, int) or k >= OWN:
                eng.wait_ge(x_loaded, k * (16 * PAIR))
            if not isinstance(k, int) or k > OWN:
                eng.wait_ge(x_biased, k)
                eng.wait_ge(xT_ps_ready, k)
            for half in halves:
                eng.dma_start(x_rows(t)[half * S:(half + 1) * S, :],
                              x[bass.ds(sample(w, half), 1), :, :].rearrange("o s h -> (o s) h")).then_inc(
                                  first_x_loaded[t] if own(t) else x_loaded, 16)

        def store_half(eng, n, half, b):
            eng.dma_start(out[bass.ds(b, 1), :, :].rearrange("o s h -> (o s) h"),
                          xs_row(n)[half * S:(half + 1) * S, :]).then_inc(stored, 16)

        def entry(eng, at, hi, lo=0):
            return eng.value_load(table[0:1, bass.ds(at, 1)], min_val=lo, max_val=hi)

        def all_blocks(eng):
            return entry(eng, T_END + E - 1, MAX_BLOCKS, B // PAIR)

        def word(eng, t, back=0):
            return entry(eng, t + (T_WORD - back), E * EXPERT - 1)

        def sample(w, half):
            return w // SECOND % B if half else w % B

        def second_there(w):
            return w // VALID % 2 > 0

        def expert(eng, w):
            return eng.snap(w // EXPERT)

        def store_block(eng, t):
            w = word(eng, t, STORE_LAG)
            eng.wait_ge(y_ready, t)
            store_half(eng, t - (STORE_LAG - 1), 0, sample(w, 0))
            with eng.If(second_there(w)):
                store_half(eng, t - (STORE_LAG - 1), 1, sample(w, 1))
            with eng.Else():
                eng.nop()

        @block.sync
        def _(sp):
            sp.dma_start(idx_i[:, :], idx.rearrange("(b o) -> b o", o=1)).then_inc(idx_loaded, 16)
            sp.dma_start(bi_rows[:, :], bi.rearrange("e (c p) -> (e c) p", p=P)).then_inc(bi_loaded, 16)
            sp.wait_ge(table_ready, 1)

            for t in range(OWN + 1):
                load_block(sp, t - 1, [0])
            load_rows(sp, bo_bc, bo, 0, E, bo_loaded)
            load_gamma_beta(sp, 0)
            load_wi(sp, 1)
            load_block(sp, 3 - 1)
            load_wo(sp, 1)
            blocks = all_blocks(sp)
            begin = 0
            for e in range(E):
                end = entry(sp, T_END + e, MAX_BLOCKS)
                stop = sp.snap(end + (end < blocks) + 1).with_bounds(min_val=1, max_val=MAX_BLOCKS + 1)
                first = PEELED - 1
                if e > 0:
                    first = sp.snap(begin + sum((begin < n) for n in range(1, PEELED)))
                with sp.If(first < stop):
                    with sp.Fori(first, stop) as k:
                        with sp.If(k > STORE_LAG - 1):
                            store_block(sp, k.with_bounds(min_val=STORE_LAG, max_val=MAX_BLOCKS))
                        with sp.Else():
                            sp.nop()
                        load_block(sp, k)
                    sp.nop()
                with sp.Else():
                    sp.nop()
                begin = stop
                if e + 2 < E:
                    load_wi(sp, e + 2)
                    load_wo(sp, e + 2)
            for more in range(1, STORE_LAG - 1):
                store_block(sp, blocks + more)
            w = word(sp, blocks, 1)
            sp.wait_ge(y_ready, blocks + (STORE_LAG - 1))
            store_half(sp, blocks, 0, sample(w, 0))
            sp.wait_ge(stored, 16 * B)

        @block.gpsimd
        def _(pool):
            nc.gpsimd.iota(expert_iota[:, :], [[1, E]], base=0, channel_multiplier=0,
                           allow_small_or_imprecise_dtypes=True).then_inc(const_step, 1)
            nc.gpsimd.iota(slot_iota[:, :], [[1, SLOTS_X]], base=0, channel_multiplier=0,
                           allow_small_or_imprecise_dtypes=True).then_inc(const_step, 1)
            nc.gpsimd.iota(sample_iota[:, :], [[0, 1]], base=0, channel_multiplier=1,
                           allow_small_or_imprecise_dtypes=True).then_inc(const_step, 1)
            nc.gpsimd.memset(ones[:, :], 1.0).then_inc(const_step, 1)
            nc.gpsimd.memset(ident[:, :], 0.0).then_inc(const_step, 1)
            nc.gpsimd.memset(minus_half[:, :], -0.5).then_inc(const_step, 1)
            pool.wait_ge(const_step, 6)
            nc.gpsimd.affine_select(out=before[:, :], in_=ones[:, :], compare_op=ALU.is_gt, fill=0.0, base=0,
                                    pattern=[[1, B]], channel_multiplier=-1).then_inc(const_step, 1)
            nc.gpsimd.affine_select(out=ident[:, :], in_=ident[:, :], compare_op=ALU.not_equal, fill=1.0, base=0,
                                    pattern=[[-1, P]], channel_multiplier=1).then_inc(const_step, 1)

            pool.wait_ge(table_ready, 1)
            def add_bo(t, loads=None):
                e = expert(pool, word(pool, t))
                if own(t):
                    pool.wait_ge(first_x_loaded[t], 16 * PAIR)
                else:
                    pool.wait_ge(x_loaded, (loads + (OWN - 1)) * (16 * PAIR))
                nc.gpsimd.tensor_tensor(xs_row(t + 1), x_rows(t),
                                        bo_bc[:, bass.ds(e, 1), :].rearrange("p o h -> p (o h)"),
                                        ALU.add).then_inc(x_biased, 1)

            blocks = all_blocks(pool)
            pool.wait_ge(bo_loaded, 16)
            for t in range(OWN + 1):
                add_bo(t, 1)
            def root(n):
                pool.wait_ge(var_ready, n)
                nc.gpsimd.tensor_tensor(rstd[:, :], var_eps[:, :], minus_half[:, :], ALU.pow).then_inc(rstd_ready, 1)

            with pool.Fori(1, blocks) as n:
                add_bo(n + 2, n + 1)
                root(n)
            root(blocks)

        @block.scalar
        def _(act):
            load_wi(act, 0)
            load_wo(act, 0)
            act.sem_inc(gelu_done, IC)
            act.sem_inc(h_used, IC)
            act.sem_inc(h_hi_done, PIECES)
            act.sem_inc(h_lo_done, PIECES)
            act.sem_inc(y_ready, STORE_LAG - 1)
            act.sem_inc(x_loaded, OWN * 16 * PAIR - 16 * PAIR)
            act.wait_ge(const_step, 8)
            nc.scalar.activation(scratch[:, :], minus_half[:, :], ACT.Gelu)
            act.wait_ge(table_ready, 1)
            for t in range(OWN + 1):
                load_block(act, t - 1, [1])

            def split_wo(e):
                act.wait_ge(wo_loaded[e % 2], 16 * (e // 2 + 1))
                if e >= 2:
                    act.wait_ge(h_used, ends_of[e - 2] * IC + IC)
                nc.scalar.activation(wo_hi[:, e % 2, :, :], wo_in[:, e % 2, :, :], ACT.Copy).then_inc(wo_hi_done, 1)

            def gelu_block(j):
                e = expert(act, word(act, j))
                for c in range(IC):
                    if c % 2 == 0:
                        act.wait_ge(preact_ready, j * IC + (c + 2))
                    if c % PER == 0:
                        act.wait_ge(h_lo_done, j * PIECES + (c // PER + 1))
                    nc.scalar.activation(h[:, c, :], preact_chunk(c), ACT.Gelu,
                                         bias=biT[:, bass.ds(e * IC + c, 1)]).then_inc(gelu_done, 1)
                for m in range(PIECES):
                    act.wait_ge(gelu_done, j * IC + (IC + (m + 1) * PER))
                    act.wait_ge(h_used, j * IC + (m + 1) * PER)
                    nc.scalar.activation(h_hi[:, m * PER:(m + 1) * PER, :], h[:, m * PER:(m + 1) * PER, :],
                                         ACT.Copy).then_inc(h_hi_done, 1)

            split_wo(0)
            act.wait_ge(biT_ready, 1)
            ends_of = []
            for e in range(E):
                begin = ends_of[e - 1] if e else 0
                ends_of.append(entry(act, T_END + e, MAX_BLOCKS))
                if e > 0:
                    split_wo(e)
                with act.If(begin < ends_of[e]):
                    with act.Fori(begin, ends_of[e]) as j:
                        gelu_block(j)
                    act.nop()
                with act.Else():
                    act.nop()
                if e % 2 == 0 and e + 2 < E:
                    load_gamma_beta(act, e + 2)
            blocks = all_blocks(act)
            w = word(act, blocks, 1)
            with act.If(second_there(w)):
                act.wait_ge(y_ready, blocks + (STORE_LAG - 1))
                store_half(act, blocks, 1, sample(w, 1))
            with act.Else():
                act.nop()

        @block.vector
        def _(dve):
            steps = [0]

            def chain(ins):
                steps[0] += 1
                ins.then_inc(sort_step, 1)
                dve.wait_ge(sort_step, steps[0])

            dve.wait_ge(idx_loaded, 16)
            dve.wait_ge(const_step, 8)
            chain(nc.vector.tensor_copy(idx_f[:, :], idx_i[:, :]))
            chain(nc.vector.tensor_scalar(onehot[:, :], expert_iota[:, :], idx_f[:, 0:1], None, ALU.is_equal))
            chain(nc.vector.scalar_tensor_tensor(code[:, 0:1], idx_f[:, :], float(EXPERT), sample_iota[:, :],
                                                 ALU.mult, ALU.add))
            chain(nc.vector.tensor_scalar(code[:, 1:2], sample_iota[:, :], float(SECOND), float(VALID),
                                          ALU.mult, ALU.add))
            dve.wait_ge(ranked, 1)
            chain(nc.vector.tensor_scalar(pairs_i[:, :], tab_ps[0:B, E:2 * E], float(PAIR - 1), None, ALU.add))
            chain(nc.vector.tensor_scalar(halved_i[:, :], pairs_i[:, :], 1, None, ALU.logical_shift_right))
            chain(nc.vector.tensor_copy(nblocks[:, :], halved_i[:, :]))
            chain(nc.vector.tensor_tensor_scan(ends[:, E:2 * E], ones[:, 0:E], nblocks[:, :], 0.0, ALU.mult, ALU.add))
            chain(nc.vector.tensor_tensor(ends[:, 0:E], ends[:, E:2 * E], nblocks[:, :], ALU.subtract))
            chain(nc.vector.scalar_tensor_tensor(place[:, :], ends[:, 0:E], float(PAIR), tab_ps[0:B, 0:E],
                                                 ALU.mult, ALU.add))
            chain(nc.vector.tensor_tensor(placed[:, :], place[:, :], onehot[:, :], ALU.mult))
            chain(nc.vector.reduce_sum(slot_of[:, :], placed[:, :], mybir.AxisListType.X))
            chain(nc.vector.tensor_scalar(perm[:, :], slot_iota[:, :], slot_of[:, 0:1], None, ALU.is_equal))
            dve.wait_ge(permuted, 1)
            chain(nc.vector.tensor_copy(table[0:1, T_BEGIN:T_WORD], ends[0:1, :]))
            nc.vector.tensor_copy(table[0:1, T_WORD:T_ALL], tab_ps[0:1, 2 * E:2 * E + TILES]).then_inc(table_ready, 1)
            dve.wait_ge(table_ready, 1)
            dve.wait_ge(biT_ps_ready, 1)
            nc.vector.tensor_copy(biT[:, :], tab_ps[:, 256:256 + E * IC]).then_inc(biT_ready, 1)

            def copy_xT(t):
                dve.wait_ge(xT_ps_ready, t + 1)
                nc.vector.tensor_copy(xT[:, bass.ds(t % 2, 1), :, :].rearrange("p o k n -> p (o k n)"),
                                      xT_ps[:, 0:H]).then_inc(xT_ready, 1)

            def layer_norm(n, e):
                dve.wait_ge(x_biased, n)
                dve.wait_ge(h_used, n * IC + IC)
                row = xs_row(n)
                nc.vector.tensor_tensor(r[:, :], sums(n), row, ALU.add).then_inc(sums_free, 1)
                dve.wait_ge(sums_free, n + 2)
                nc.vector.bn_stats(stats[:, :], r[:, :]).then_inc(ln_step, 1)
                dve.wait_ge(ln_step, n * LN_STEPS + 1)
                dve.sem_inc(ln_step, 1)
                nc.vector.bn_aggr(meanvar[:, :], stats[:, :]).then_inc(ln_step, 1)
                dve.wait_ge(ln_step, n * LN_STEPS + 3)
                nc.vector.tensor_scalar(var_eps[:, :], meanvar[:, 1:2], LN_EPS, None, ALU.add).then_inc(var_ready, 1)
                nc.vector.scalar_tensor_tensor(centred[:, :], r[:, :], meanvar[:, 0:1],
                                               gamma_bc[:, bass.ds(e, 1), :].rearrange("p o h -> p (o h)"),
                                               ALU.subtract, ALU.mult).then_inc(ln_step, 1)
                dve.wait_ge(ln_step, n * LN_STEPS + 4)
                dve.wait_ge(rstd_ready, n)
                nc.vector.scalar_tensor_tensor(row, centred[:, :], rstd[:, 0:1],
                                               beta_bc[:, bass.ds(e, 1), :].rearrange("p o h -> p (o h)"),
                                               ALU.mult, ALU.add).then_inc(y_ready, 1)

            blocks = all_blocks(dve)
            very_last_expert = expert(dve, word(dve, blocks, 1))
            ends_of = [entry(dve, T_END + e, MAX_BLOCKS) for e in range(E // 2)]
            dve.sem_inc(sums_free, 2)
            dve.sem_inc(ln_step, LN_STEPS)

            def split_wo(e):
                dve.wait_ge(wo_hi_done, e + 1)
                nc.vector.tensor_tensor(wo_lo[:, e % 2, :, :], wo_in[:, e % 2, :, :],
                                        wo_hi[:, e % 2, :, :].bitcast(FP32), ALU.subtract).then_inc(wo_lo_done, 1)

            def split_h(j):
                for m in range(PIECES):
                    dve.wait_ge(h_hi_done, j * PIECES + (PIECES + m + 1))
                    nc.vector.tensor_tensor(h_lo[:, m * PER:(m + 1) * PER, :], h[:, m * PER:(m + 1) * PER, :],
                                            h_hi[:, m * PER:(m + 1) * PER, :].bitcast(FP32),
                                            ALU.subtract).then_inc(h_lo_done, 1)

            for t in range(OWN):
                copy_xT(t)
            split_wo(0)
            ends_of += [entry(dve, T_END + e, MAX_BLOCKS) for e in range(E // 2, E)]
            for e in range(E):
                begin, end = ends_of[e - 1] if e else 0, ends_of[e]
                if e > 0:
                    split_wo(e)
                if e % 2 == 0:
                    dve.wait_ge(rows_loaded[e // 2], 16 * 2)
                with dve.If(begin < end):
                    with dve.Fori(begin, end) as j:
                        last_expert = expert(dve, word(dve, j, 1))
                        copy_xT(j + 2)
                        split_h(j)
                        with dve.If(j > 0):
                            layer_norm(j, last_expert)
                        with dve.Else():
                            dve.nop()
                    dve.nop()
                with dve.Else():
                    dve.nop()
            layer_norm(blocks, very_last_expert)

        @block.tensor
        def _(pe):
            pe.wait_ge(const_step, 8)
            pe.wait_ge(sort_step, 2)
            nc.tensor.matmul(tab_ps[0:B, 0:E], before[:, :], onehot[:, :], start=True, stop=True)
            nc.tensor.matmul(tab_ps[0:B, E:2 * E], ones[:, :], onehot[:, :], start=True, stop=True).then_inc(ranked, 1)
            pe.wait_ge(sort_step, 13)
            for half in range(PAIR):
                last = nc.tensor.matmul(tab_ps[0:1, 2 * E:2 * E + TILES], code[:, half:half + 1],
                                        perm[:, :].rearrange("b (t s) -> b s t", s=PAIR)[:, half, :],
                                        start=(half == 0), stop=(half == PAIR - 1))
            last.then_inc(permuted, 1)
            pe.wait_ge(bi_loaded, 16)
            pe.wait_ge(table_ready, 1)
            nc.tensor.transpose(tab_ps[:, 256:256 + E * IC], bi_rows[:, :],
                                ident[0:E * IC, 0:E * IC]).then_inc(biT_ps_ready, 1)
            for _ in range(WARM_UP):
                nc.tensor.matmul(preact_chunk(0), ident[:, :], ident[:, :], start=True, stop=True)

            def transpose_from(buffer):
                for k in range(HC):
                    last = nc.tensor.transpose(xT_ps[:, k * P:(k + 1) * P],
                                               x_in[:, buffer, k * P:(k + 1) * P], ident[:, :])
                last.then_inc(xT_ps_ready, 1)

            def transpose_x(t, loads=None):
                if own(t):
                    pe.wait_ge(first_x_loaded[t], 16 * PAIR)
                else:
                    pe.wait_ge(x_loaded, (loads + (OWN - 1)) * (16 * PAIR))
                if not isinstance(t, int) or t > 0:
                    pe.wait_ge(xT_ready, t)
                if own(t):
                    transpose_from(x_buffer(t))
                else:
                    with pe.If(t % 2 > 0):
                        transpose_from(1)
                    with pe.Else():
                        transpose_from(0)

            def first_product(j, e):
                pe.wait_ge(xT_ready, j + 1)
                for c in range(IC):
                    if c % 2 == 0:
                        pe.wait_ge(gelu_done, j * IC + (c + 2))
                    for k in range(HC):
                        last = nc.tensor.matmul(preact_chunk(c), wi[:, e, k, c * P:(c + 1) * P],
                                                xT[:, bass.ds(j % 2, 1), k, :].rearrange("p o n -> p (o n)"),
                                                start=(k == 0), stop=(k == HC - 1))
                    last.then_inc(preact_ready, 1)

            def second_product(n, e):
                into = sums(n)
                pe.wait_ge(sums_free, n)
                pe.wait_ge(wo_lo_done, e + 1)
                for m in range(PIECES):
                    chunks = range(m * PER, (m + 1) * PER)
                    pe.wait_ge(h_hi_done, n * PIECES + (m + 1))
                    for c in chunks:
                        for w in (wo_hi, wo_lo):
                            nc.tensor.matmul(into, h_hi[:, c, :], w[:, e % 2, c, :],
                                             start=(c == 0 and w is wo_hi), stop=False)
                    pe.wait_ge(h_lo_done, n * PIECES + (m + 1))
                    for c in chunks:
                        nc.tensor.matmul(into, h_lo[:, c, :], wo_hi[:, e % 2, c, :],
                                         start=False, stop=(c == IC - 1)).then_inc(h_used, 1)

            transpose_x(0)
            transpose_x(1)
            last_begin, begin, end = 0, 0, entry(pe, T_END, MAX_BLOCKS)

            def second_product_of_last_expert(n, e):
                if e > 0:
                    with pe.If(last_begin < begin):
                        second_product(n, e - 1)
                    with pe.Else():
                        pe.nop()

            for e in range(E):
                if e > 0:
                    last_begin, begin, end = begin, end, entry(pe, T_END + e, MAX_BLOCKS)
                with pe.If(begin < end):
                    pe.wait_ge(wi_loaded[e], 16)
                    with pe.Fori(begin, end) as j:
                        first_product(j, e)
                        transpose_x(j + 2, j + 1)
                        with pe.If(j > begin):
                            second_product(j, e)
                        with pe.Else():
                            second_product_of_last_expert(j, e)
                            pe.nop()
                    pe.nop()
                with pe.Else():
                    second_product_of_last_expert(begin, e)
                    pe.nop()
            last_begin, begin = begin, end
            second_product_of_last_expert(begin, E)


INPUTS = ["x", "itok_B_0_7", "L0_cond_Wi", "L0_cond_bi", "L0_cond_Wo", "L0_cond_bo", "L0_cond_gamma", "L0_cond_beta"]


def kernel(**inputs):
    import numpy as np
    import concourse.bacc as bacc
    from concourse.bass_utils import run_bass_kernel_spmd

    nc = bacc.Bacc("TRN2", target_bir_lowering=False, num_devices=1)
    arrays, args = {}, []
    for name in INPUTS:
        a = np.ascontiguousarray(inputs[name])
        arrays[name + "_dram"] = a
        args.append(nc.dram_tensor(name + "_dram", a.shape, mybir.dt.from_np(a.dtype), kind="ExternalInput").ap())
    y = nc.dram_tensor("y_dram", inputs["x"].shape, FP32, kind="ExternalOutput").ap()
    expert_ffn(nc, *args, y)
    result = run_bass_kernel_spmd(nc, [arrays], core_ids=[0])
    return result.results[0]["y_dram"]
```

```python
from contextlib import ExitStack

import concourse.bass as bass
from concourse import mybir

FP32 = mybir.dt.float32
FP32R = mybir.dt.float32r
I32 = mybir.dt.int32
ALU = mybir.AluOpType
ACT = mybir.ActivationFunctionType

P = 128
LN_EPS = 1e-12


def expert_ffn(nc, x, idx, Wi, bi, Wo, bo, gamma, beta, out):
    B, S, H = x.shape
    E, _, I = Wi.shape
    TILE = P // S
    QUAD = 2 * TILE
    N = QUAD * S
    HC, IC = H // P, I // P
    MAX_BLOCKS = (B + (QUAD - 1) * E) // QUAD
    BLOCKS = MAX_BLOCKS + 1
    STORE_LAG = 5
    WARM_UP = 12
    PIECES = 4
    PER = 2 * IC // PIECES
    LN_STEPS = 7
    assert TILE == 2
    T_BEGIN, T_END, T_WORD = 0, E, 2 * E
    SECOND = B
    THERE = (B * B, 2 * B * B)
    EXPERT = 4 * B * B
    T_ALL = T_WORD + 2 * BLOCKS

    ctx = ExitStack()
    with ctx:
        def sb(name, shape, dt=FP32):
            return ctx.enter_context(nc.sbuf_tensor(name, shape, dt))

        def pb(name, shape, dt=FP32):
            return ctx.enter_context(nc.psum_tensor(name, shape, dt))

        def sem(name):
            return ctx.enter_context(nc.semaphore(name))

        wi_in = sb("wi_in", [P, 2, HC, I])
        wi_hi = sb("wi_hi", [P, 2, HC, I], FP32R)
        wi_lo = sb("wi_lo", [P, 2, HC, I], FP32R)
        wo_in = sb("wo_in", [P, 2, IC, H])
        wo_hi = sb("wo_hi", [P, 2, IC, H], FP32R)
        wo_lo = sb("wo_lo", [P, 2, IC, H], FP32R)
        x_in = sb("x_in", [P, 2, 2, H])
        xs = sb("xs", [P, BLOCKS + 1, 2, H])
        xT_hi = sb("xT_hi", [P, HC, N], FP32R)
        xT_lo = sb("xT_lo", [P, HC, N], FP32R)
        h = sb("h", [P, IC, N])
        h_hi = sb("h_hi", [P, IC, N], FP32R)
        h_lo = sb("h_lo", [P, IC, N], FP32R)
        biT = sb("biT", [P, E * IC])
        bi_rows = sb("bi_rows", [E * IC, P])
        bo_bc = sb("bo_bc", [P, E, H])
        gamma_bc = sb("gamma_bc", [P, E, H])
        beta_bc = sb("beta_bc", [P, E, H])
        ident = sb("ident", [P, P])
        r = sb("r", [P, 2, H])
        centred = sb("centred", [P, 2, H])
        stats = sb("stats", [P, 2, 6])
        meanvar = sb("meanvar", [P, 2, 2])
        var_eps = sb("var_eps", [P, 2])
        minus_half = sb("minus_half", [P, 2])
        rstd = sb("rstd", [P, 2])
        gelu_of_any = sb("gelu_of_any", [P, 2])
        idx_i = sb("idx_i", [B, 1], I32)
        idx_f = sb("idx_f", [B, 1])
        expert_iota = sb("expert_iota", [B, E])
        slot_iota = sb("slot_iota", [B, 2 * TILE * BLOCKS])
        sample_iota = sb("sample_iota", [B, 1])
        before = sb("before", [B, B])
        ones = sb("ones", [B, B])
        onehot = sb("onehot", [B, E])
        padded_i = sb("padded_i", [B, E], I32)
        blocks_i = sb("blocks_i", [B, E], I32)
        nblocks = sb("nblocks", [B, E])
        ends = sb("ends", [B, 2 * E])
        place = sb("place", [B, E])
        placed = sb("placed", [B, E])
        slot_of = sb("slot_of", [B, 1])
        code = sb("code", [B, TILE])
        flagged = sb("flagged", [B, 1])
        perm = sb("perm", [B, 2 * TILE * BLOCKS])
        table = sb("table", [1, T_ALL], I32)

        preact = pb("preact", [P, IC // 2, 512])
        sums_ps = pb("sums_ps", [P, 2, 512])
        xT_ps = pb("xT_ps", [P, 512])
        tab_ps = pb("tab_ps", [P, 512])

        def xs_rows(n, tile):
            return xs[:, bass.ds(n, 1), tile, :].rearrange("p o h -> p (o h)")

        def sums(tile):
            return sums_ps[:, tile, 0:H]

        def preact_chunk(c):
            return preact[:, c // 2, (c % 2) * N:(c % 2 + 1) * N]

        def wo_half(part, e, half):
            return part[:, e % 2, half * PER:(half + 1) * PER, :]

        def piece(part, i):
            tile, half = i // 2, i % 2
            return part[:, half * PER:(half + 1) * PER, tile * P:(tile + 1) * P]

        idx_loaded = sem("idx_loaded")
        bi_loaded = sem("bi_loaded")
        bo_loaded = sem("bo_loaded")
        rows_loaded = [sem(f"rows_loaded{e}") for e in range(0, E, 2)]
        wi_loaded = [sem(f"wi_loaded{e}") for e in range(E)]
        wo_loaded = [sem(f"wo_loaded{s}") for s in range(2)]
        first_wi_hi_done = sem("first_wi_hi_done")
        wi_hi_done = sem("wi_hi_done")
        wi_lo_done = sem("wi_lo_done")
        wo_hi_done = sem("wo_hi_done")
        wo_lo_done = sem("wo_lo_done")
        last_wo_lo_done = sem("last_wo_lo_done")
        first_x_loaded = sem("first_x_loaded")
        x_loaded = sem("x_loaded")
        const_step = sem("const_step")
        sort_step = sem("sort_step")
        ranked = sem("ranked")
        permuted = sem("permuted")
        table_ready = sem("table_ready")
        biT_ps_ready = sem("biT_ps_ready")
        biT_ready = sem("biT_ready")
        xT_ps_ready = sem("xT_ps_ready")
        xT_hi_done = sem("xT_hi_done")
        xT_ready = sem("xT_ready")
        preact_ready = sem("preact_ready")
        gelu_done = sem("gelu_done")
        h_hi_done = sem("h_hi_done")
        h_lo_done = sem("h_lo_done")
        h_used = sem("h_used")
        x_biased = sem("x_biased")
        sums_free = sem("sums_free")
        ln_step = sem("ln_step")
        var_ready = sem("var_ready")
        rstd_ready = sem("rstd_ready")
        y_ready = sem("y_ready")
        stored = sem("stored")

        block = ctx.enter_context(nc.Block())

        def load_wi(eng, e):
            if e >= 2:
                eng.wait_ge(wi_lo_done, e - 1)
            eng.dma_start(wi_in[:, e % 2, :, :], Wi[e, :, :].rearrange("(k p) n -> p k n", p=P)).then_inc(wi_loaded[e], 16)

        def load_wo(eng, e):
            if e >= 2:
                eng.wait_ge(wo_lo_done, 2 * (e - 1))
            eng.dma_start(wo_in[:, e % 2, :, :], Wo[e, :, :].rearrange("(c p) n -> p c n", p=P)).then_inc(wo_loaded[e % 2], 16)

        def load_rows(eng, dst, src, e0, e1, done):
            eng.dma_start(dst[:, e0:e1, :].rearrange("p e h -> p (e h)"),
                          src[e0:e1, :].rearrange("e h -> (e h)").partition_broadcast(P)).then_inc(done, 16)

        def load_gamma_beta(eng, e):
            load_rows(eng, gamma_bc, gamma, e, e + 2, rows_loaded[e // 2])
            load_rows(eng, beta_bc, beta, e, e + 2, rows_loaded[e // 2])

        def is_first(t):
            return isinstance(t, int) and t == 0

        def x_tile(t, tile):
            return x_in[:, 1 if is_first(t) else 0, tile, :]

        def load_block(eng, t, tiles=(0, 1)):
            words = {tile: word(eng, t, tile) for tile in tiles}
            samples = samples_of(eng, words)
            if not isinstance(t, int):
                eng.wait_ge(x_biased, t * 2)
                eng.wait_ge(xT_ps_ready, t)
            for (tile, half), b in samples.items():
                eng.dma_start(x_tile(t, tile)[half * S:(half + 1) * S, :],
                              x[bass.ds(b, 1), :, :].rearrange("o s h -> (o s) h")).then_inc(
                                  first_x_loaded if is_first(t) else x_loaded, 16)

        def store_half(eng, n, tile, half, b):
            eng.dma_start(out[bass.ds(b, 1), :, :].rearrange("o s h -> (o s) h"),
                          xs_rows(n, tile)[half * S:(half + 1) * S, :]).then_inc(stored, 16)

        def entry(eng, at, hi, lo=0):
            return eng.value_load(table[0:1, bass.ds(at, 1)], min_val=lo, max_val=hi)

        def all_blocks(eng):
            return entry(eng, T_END + E - 1, MAX_BLOCKS, B // QUAD)

        def word(eng, t, tile, back=0):
            return entry(eng, t * 2 + (T_WORD + tile - 2 * back), E * EXPERT - 1)

        def sample(w, half):
            return w // SECOND % B if half else w % B

        def expert(eng, w):
            return eng.snap(w // EXPERT)

        def samples_of(eng, words):
            return {(tile, half): eng.snap(sample(w, half)) for tile, w in words.items() for half in range(TILE)}

        def store_those_there(eng, n, samples, there):
            for (tile, half), b in samples.items():
                with eng.If(there(tile, half) > 0):
                    store_half(eng, n, tile, half, b)
                with eng.Else():
                    eng.nop()

        def store_block(eng, t):
            words = {tile: word(eng, t, tile, STORE_LAG) for tile in range(2)}
            samples = samples_of(eng, words)
            all_there = eng.snap(words[1] // THERE[1] % 2)
            eng.wait_ge(y_ready, t * 2)
            n = t - (STORE_LAG - 1)
            with eng.If(all_there > 0):
                for (tile, half), b in samples.items():
                    store_half(eng, n, tile, half, b)
            with eng.Else():
                store_those_there(eng, n, samples, lambda tile, half: words[tile] // THERE[half] % 2)

        def store_last_tile(eng, blocks, tile):
            w = word(eng, blocks, tile, 1)
            samples = samples_of(eng, {tile: w})
            there = [eng.snap(w // THERE[half] % 2) for half in range(TILE)]
            eng.wait_ge(y_ready, blocks * 2 + (2 * STORE_LAG - 3 + tile))
            store_those_there(eng, blocks, samples, lambda tile, half: there[half])

        @block.sync
        def _(sp):
            sp.dma_start(idx_i[:, :], idx.rearrange("(b o) -> b o", o=1)).then_inc(idx_loaded, 16)
            sp.dma_start(bi_rows[:, :], bi.rearrange("e (c p) -> (e c) p", p=P)).then_inc(bi_loaded, 16)
            sp.wait_ge(table_ready, 1)

            load_block(sp, 0, [0])
            load_wi(sp, 1)
            load_block(sp, 1, [0])
            load_rows(sp, bo_bc, bo, 0, E, bo_loaded)
            load_gamma_beta(sp, 0)
            load_wi(sp, 2)
            blocks = all_blocks(sp)
            begin = 0
            for e in range(E):
                end = entry(sp, T_END + e, MAX_BLOCKS)
                stop = sp.snap(end + (end < blocks) + 1).with_bounds(min_val=1, max_val=MAX_BLOCKS + 1)
                first = 2
                if e > 0:
                    first = sp.snap(begin + sum((begin < n) for n in range(1, 3)))
                with sp.If(first < stop):
                    with sp.Fori(first, stop) as t:
                        with sp.If(t > STORE_LAG - 1):
                            store_block(sp, t.with_bounds(min_val=STORE_LAG, max_val=MAX_BLOCKS))
                        with sp.Else():
                            sp.nop()
                        load_block(sp, t)
                    sp.nop()
                with sp.Else():
                    sp.nop()
                begin = stop
                if e == 0:
                    load_wo(sp, 1)
                    load_wi(sp, 3)
            for more in range(1, STORE_LAG - 1):
                store_block(sp, blocks + more)
            store_last_tile(sp, blocks, 0)
            sp.wait_ge(stored, 16 * B)

        @block.gpsimd
        def _(pool):
            nc.gpsimd.iota(expert_iota[:, :], [[1, E]], base=0, channel_multiplier=0,
                           allow_small_or_imprecise_dtypes=True).then_inc(const_step, 1)
            nc.gpsimd.iota(slot_iota[:, :], [[1, 2 * TILE * BLOCKS]], base=0, channel_multiplier=0,
                           allow_small_or_imprecise_dtypes=True).then_inc(const_step, 1)
            nc.gpsimd.iota(sample_iota[:, :], [[0, 1]], base=0, channel_multiplier=1,
                           allow_small_or_imprecise_dtypes=True).then_inc(const_step, 1)
            nc.gpsimd.memset(ones[:, :], 1.0).then_inc(const_step, 1)
            nc.gpsimd.memset(ident[:, :], 0.0).then_inc(const_step, 1)
            nc.gpsimd.memset(minus_half[:, :], -0.5).then_inc(const_step, 1)
            pool.wait_ge(const_step, 6)
            nc.gpsimd.affine_select(out=before[:, :], in_=ones[:, :], compare_op=ALU.is_gt, fill=0.0, base=0,
                                    pattern=[[1, B]], channel_multiplier=-1).then_inc(const_step, 1)
            nc.gpsimd.affine_select(out=ident[:, :], in_=ident[:, :], compare_op=ALU.not_equal, fill=1.0, base=0,
                                    pattern=[[-1, P]], channel_multiplier=1).then_inc(const_step, 1)

            pool.wait_ge(table_ready, 1)

            def split_wo(e):
                pool.wait_ge(wo_hi_done, e + 1)
                for half in range(0 if e < E - 1 else 1, 2):
                    nc.gpsimd.tensor_tensor(wo_half(wo_lo, e, half), wo_half(wo_in, e, half),
                                            wo_half(wo_hi, e, half).bitcast(FP32),
                                            ALU.subtract).then_inc(wo_lo_done, 1)

            def add_bo(t):
                e = expert(pool, word(pool, t, 0))
                if is_first(t):
                    pool.wait_ge(first_x_loaded, 16 * QUAD)
                else:
                    pool.wait_ge(x_loaded, t * (16 * QUAD))
                for tile in range(2):
                    nc.gpsimd.tensor_tensor(xs_rows(t + 1, tile), x_tile(t, tile),
                                            bo_bc[:, bass.ds(e, 1), :].rearrange("p o h -> p (o h)"),
                                            ALU.add).then_inc(x_biased, 1)

            def root(n):
                pool.wait_ge(var_ready, n + 1)
                nc.gpsimd.tensor_tensor(rstd[:, :], var_eps[:, :], minus_half[:, :], ALU.pow).then_inc(rstd_ready, 1)

            blocks = all_blocks(pool)
            ends_of = [entry(pool, T_END + e, MAX_BLOCKS) for e in range(E)]
            split_wo(0)
            pool.wait_ge(bo_loaded, 16)
            add_bo(0)
            add_bo(1)
            for e in range(E):
                begin = ends_of[e - 1] if e else 0
                with pool.If(begin < ends_of[e]):
                    with pool.Fori(begin, ends_of[e]) as j:
                        with pool.If(j > 0):
                            add_bo(j + 1)
                        with pool.Else():
                            pool.nop()
                        if e > 0:
                            with pool.If(j > begin):
                                pool.nop()
                            with pool.Else():
                                split_wo(e)
                        with pool.If(j > 0):
                            root(j)
                        with pool.Else():
                            pool.nop()
                    pool.nop()
                with pool.Else():
                    if 0 < e < E - 1:
                        split_wo(e)
                    pool.nop()
            root(blocks)

        @block.scalar
        def _(act):
            load_wi(act, 0)
            load_wo(act, 0)
            act.sem_inc(gelu_done, IC)
            act.sem_inc(h_used, 2 * IC)
            act.sem_inc(preact_ready, IC)
            act.sem_inc(var_ready, 1)
            act.sem_inc(rstd_ready, 1)
            act.sem_inc(h_hi_done, PIECES)
            act.sem_inc(h_lo_done, PIECES)
            act.sem_inc(y_ready, 2 * STORE_LAG - 2)
            act.wait_ge(const_step, 8)
            nc.scalar.activation(gelu_of_any[:, :], minus_half[:, :], ACT.Gelu)
            act.wait_ge(table_ready, 1)
            load_block(act, 0, [1])

            def split_wi(e):
                act.wait_ge(wi_loaded[e], 16)
                if e >= 2:
                    act.wait_ge(preact_ready, ends_of[e - 2] * IC + IC)
                nc.scalar.activation(wi_hi[:, e % 2, :, :], wi_in[:, e % 2, :, :], ACT.Copy).then_inc(wi_hi_done, 1)

            def split_wo(e):
                act.wait_ge(wo_loaded[e % 2], 16 * (e // 2 + 1))
                if e >= 2:
                    act.wait_ge(h_used, ends_of[e - 2] * (2 * IC) + 2 * IC)
                nc.scalar.activation(wo_hi[:, e % 2, :, :], wo_in[:, e % 2, :, :], ACT.Copy).then_inc(wo_hi_done, 1)

            def gelu_block(j):
                e = expert(act, word(act, j, 0))
                for c in range(IC):
                    if c % 2 == 0:
                        act.wait_ge(preact_ready, j * IC + (IC + c + 2))
                    if c % PER == 0:
                        act.wait_ge(h_lo_done, j * PIECES + (PIECES // 2 + c // PER + 1))
                    nc.scalar.activation(h[:, c, :], preact_chunk(c), ACT.Gelu,
                                         bias=biT[:, bass.ds(e * IC + c, 1)]).then_inc(gelu_done, 1)

            def split_h(j):
                for i in range(PIECES):
                    act.wait_ge(gelu_done, j * IC + (IC + (i % 2 + 1) * PER))
                    act.wait_ge(h_used, j * (2 * IC) + (i + 1) * PER)
                    nc.scalar.activation(piece(h_hi, i), piece(h, i), ACT.Copy).then_inc(h_hi_done, 1)

            load_block(act, 1, [1])
            split_wo(0)
            split_wi(1)

            def split_weights(e):
                if e + 1 < E:
                    split_wi(e + 1)
                split_wo(e)
                if e + 1 < E:
                    load_wo(act, e + 1)

            act.wait_ge(biT_ready, 1)
            ends_of = []
            for e in range(E):
                begin = ends_of[e - 1] if e else 0
                ends_of.append(entry(act, T_END + e, MAX_BLOCKS))
                with act.If(begin < ends_of[e]):
                    with act.Fori(begin, ends_of[e]) as j:
                        gelu_block(j)
                        if e > 0:
                            with act.If(j > begin):
                                act.nop()
                            with act.Else():
                                split_weights(e)
                        split_h(j)
                    act.nop()
                with act.Else():
                    if e > 0:
                        split_weights(e)
                    act.nop()
                if 0 < e < E - 3:
                    load_wi(act, e + 3)
                if e % 2 == 0 and e + 2 < E:
                    load_gamma_beta(act, e + 2)
            blocks = all_blocks(act)
            store_last_tile(act, blocks, 1)

        @block.vector
        def _(dve):
            steps = [0]

            def chain(ins):
                steps[0] += 1
                ins.then_inc(sort_step, 1)
                dve.wait_ge(sort_step, steps[0])

            dve.wait_ge(idx_loaded, 16)
            dve.wait_ge(const_step, 8)
            chain(nc.vector.tensor_copy(idx_f[:, :], idx_i[:, :]))
            chain(nc.vector.tensor_scalar(onehot[:, :], expert_iota[:, :], idx_f[:, 0:1], None, ALU.is_equal))
            chain(nc.vector.tensor_scalar(flagged[:, :], sample_iota[:, :], float(THERE[0]), None, ALU.add))
            chain(nc.vector.scalar_tensor_tensor(code[:, 0:1], idx_f[:, :], float(EXPERT), flagged[:, :],
                                                 ALU.mult, ALU.add))
            chain(nc.vector.tensor_scalar(code[:, 1:2], sample_iota[:, :], float(SECOND), float(THERE[1]),
                                          ALU.mult, ALU.add))
            dve.wait_ge(ranked, 1)
            chain(nc.vector.tensor_scalar(padded_i[:, :], tab_ps[0:B, E:2 * E], float(QUAD - 1), None, ALU.add))
            chain(nc.vector.tensor_scalar(blocks_i[:, :], padded_i[:, :], QUAD.bit_length() - 1, None, ALU.logical_shift_right))
            chain(nc.vector.tensor_copy(nblocks[:, :], blocks_i[:, :]))
            chain(nc.vector.tensor_tensor_scan(ends[:, E:2 * E], ones[:, 0:E], nblocks[:, :], 0.0, ALU.mult, ALU.add))
            chain(nc.vector.tensor_tensor(ends[:, 0:E], ends[:, E:2 * E], nblocks[:, :], ALU.subtract))
            chain(nc.vector.scalar_tensor_tensor(place[:, :], ends[:, 0:E], float(QUAD), tab_ps[0:B, 0:E],
                                                 ALU.mult, ALU.add))
            chain(nc.vector.scalar_tensor_tensor(placed[:, :], place[:, :], 1.0, onehot[:, :],
                                                 ALU.mult, ALU.mult, accum_out=slot_of[:, :]))
            chain(nc.vector.tensor_scalar(perm[:, :], slot_iota[:, :], slot_of[:, 0:1], None, ALU.is_equal))
            chain(nc.vector.tensor_copy(table[0:1, T_BEGIN:T_WORD], ends[0:1, :]))
            dve.wait_ge(permuted, 1)
            nc.vector.tensor_copy(table[0:1, T_WORD:T_ALL], tab_ps[0:1, 2 * E:2 * E + 2 * BLOCKS]).then_inc(table_ready, 1)
            dve.wait_ge(table_ready, 1)
            dve.wait_ge(biT_ps_ready, 1)
            nc.vector.tensor_copy(biT[:, :], tab_ps[:, 256:256 + E * IC]).then_inc(biT_ready, 1)

            def split_xT(t):
                dve.wait_ge(xT_ps_ready, t + 1)
                transposed = xT_ps[:, 0:HC * N].rearrange("p (k n) -> p k n", k=HC)
                nc.vector.tensor_copy(xT_hi[:, :, :], transposed).then_inc(xT_hi_done, 1)
                dve.wait_ge(xT_hi_done, t + 1)
                nc.vector.tensor_tensor(xT_lo[:, :, :], transposed, xT_hi[:, :, :].bitcast(FP32),
                                        ALU.subtract).then_inc(xT_ready, 1)

            def take_sums(n, tile):
                q = n * 2 + tile
                dve.wait_ge(x_biased, n * 2)
                dve.wait_ge(h_used, q * IC + IC)
                nc.vector.tensor_tensor(r[:, tile, :], sums(tile), xs_rows(n, tile), ALU.add).then_inc(sums_free, 1)

            def normalise(n, e):
                dve.wait_ge(sums_free, n * 2 + 3)
                for tile in range(2):
                    nc.vector.bn_stats(stats[:, tile, :], r[:, tile, :]).then_inc(ln_step, 1)
                dve.wait_ge(ln_step, n * LN_STEPS + 2)
                dve.sem_inc(ln_step, 1)
                for tile in range(2):
                    nc.vector.bn_aggr(meanvar[:, tile, :], stats[:, tile, :]).then_inc(ln_step, 1)
                dve.wait_ge(ln_step, n * LN_STEPS + 5)
                nc.vector.tensor_scalar(var_eps[:, :], meanvar[:, :, 1], LN_EPS, None, ALU.add).then_inc(var_ready, 1)
                for tile in range(2):
                    nc.vector.scalar_tensor_tensor(centred[:, tile, :], r[:, tile, :], meanvar[:, tile, 0:1],
                                                   gamma_bc[:, bass.ds(e, 1), :].rearrange("p o h -> p (o h)"),
                                                   ALU.subtract, ALU.mult).then_inc(ln_step, 1)
                dve.wait_ge(ln_step, n * LN_STEPS + 7)
                dve.wait_ge(rstd_ready, n + 1)
                for tile in range(2):
                    nc.vector.scalar_tensor_tensor(xs_rows(n, tile), centred[:, tile, :], rstd[:, tile:tile + 1],
                                                   beta_bc[:, bass.ds(e, 1), :].rearrange("p o h -> p (o h)"),
                                                   ALU.mult, ALU.add).then_inc(y_ready, 1)

            def split_wi(e):
                if e > 0:
                    dve.wait_ge(wi_hi_done, e)
                else:
                    dve.wait_ge(first_wi_hi_done, 1)
                nc.vector.tensor_tensor(wi_lo[:, e % 2, :, :], wi_in[:, e % 2, :, :],
                                        wi_hi[:, e % 2, :, :].bitcast(FP32), ALU.subtract).then_inc(wi_lo_done, 1)

            dve.wait_ge(wi_loaded[0], 16)
            nc.vector.tensor_copy(wi_hi[:, 0, :, :], wi_in[:, 0, :, :]).then_inc(first_wi_hi_done, 1)
            split_wi(0)
            blocks = all_blocks(dve)
            very_last_expert = expert(dve, word(dve, blocks, 0, 1))
            ends_of = [entry(dve, T_END + e, MAX_BLOCKS) for e in range(E // 2)]
            dve.sem_inc(sums_free, 3)
            dve.sem_inc(ln_step, LN_STEPS)

            def split_last_wo():
                dve.wait_ge(wo_hi_done, E)
                nc.vector.tensor_tensor(wo_half(wo_lo, E - 1, 0), wo_half(wo_in, E - 1, 0),
                                        wo_half(wo_hi, E - 1, 0).bitcast(FP32), ALU.subtract).then_inc(last_wo_lo_done, 1)

            def split_h(j, pieces):
                for i in pieces:
                    dve.wait_ge(h_hi_done, j * PIECES + (PIECES + i + 1))
                    nc.vector.tensor_tensor(piece(h_lo, i), piece(h, i), piece(h_hi, i).bitcast(FP32),
                                            ALU.subtract).then_inc(h_lo_done, 1)

            split_xT(0)
            ends_of += [entry(dve, T_END + e, MAX_BLOCKS) for e in range(E // 2, E)]
            split_wi(1)
            for e in range(E):
                begin, end = ends_of[e - 1] if e else 0, ends_of[e]
                with dve.If(begin < end):
                    with dve.Fori(begin, end) as j:
                        last_expert = expert(dve, word(dve, j, 0, 1))
                        if e < E - 1:
                            split_xT(j + 1)
                        else:
                            with dve.If(j + 1 < end):
                                split_xT(j + 1)
                            with dve.Else():
                                dve.nop()
                        if 0 < e < E - 1:
                            with dve.If(j > begin):
                                dve.nop()
                            with dve.Else():
                                split_wi(e + 1)
                        if e == E - 1:
                            with dve.If(j > begin):
                                dve.nop()
                            with dve.Else():
                                split_last_wo()
                        dve.wait_ge(rows_loaded[e // 2], 16 * 2)
                        with dve.If(j > 0):
                            take_sums(j, 0)
                        with dve.Else():
                            dve.nop()
                        split_h(j, (0, 1))
                        with dve.If(j > 0):
                            take_sums(j, 1)
                            split_h(j, (2, 3))
                            normalise(j, last_expert)
                        with dve.Else():
                            split_h(j, (2, 3))
                    dve.nop()
                with dve.Else():
                    if 0 < e < E - 1:
                        split_wi(e + 1)
                    dve.nop()
            for tile in range(2):
                take_sums(blocks, tile)
            normalise(blocks, very_last_expert)

        @block.tensor
        def _(pe):
            pe.wait_ge(const_step, 8)
            pe.wait_ge(sort_step, 2)
            nc.tensor.matmul(tab_ps[0:B, 0:E], before[:, :], onehot[:, :], start=True, stop=True)
            nc.tensor.matmul(tab_ps[0:B, E:2 * E], ones[:, :], onehot[:, :], start=True, stop=True).then_inc(ranked, 1)
            pe.wait_ge(sort_step, 13)
            for half in range(TILE):
                last = nc.tensor.matmul(tab_ps[0:1, 2 * E:2 * E + 2 * BLOCKS], code[:, half:half + 1],
                                        perm[:, :].rearrange("b (t s) -> b s t", s=TILE)[:, half, :],
                                        start=(half == 0), stop=(half == TILE - 1))
            last.then_inc(permuted, 1)
            pe.wait_ge(bi_loaded, 16)
            pe.wait_ge(table_ready, 1)
            nc.tensor.transpose(tab_ps[:, 256:256 + E * IC], bi_rows[:, :],
                                ident[0:E * IC, 0:E * IC]).then_inc(biT_ps_ready, 1)
            for _ in range(WARM_UP):
                nc.tensor.matmul(preact[:, 0, 0:P], ident[:, :], ident[:, :], start=True, stop=True)

            def transpose_x(t):
                if is_first(t):
                    pe.wait_ge(first_x_loaded, 16 * QUAD)
                else:
                    pe.wait_ge(x_loaded, t * (16 * QUAD))
                    pe.wait_ge(xT_ready, t)
                for k in range(HC):
                    for tile in range(2):
                        at = k * N + tile * P
                        last = nc.tensor.transpose(xT_ps[:, at:at + P], x_tile(t, tile)[:, k * P:(k + 1) * P],
                                                   ident[:, :])
                last.then_inc(xT_ps_ready, 1)

            def first_product(j, e):
                pe.wait_ge(xT_ready, j + 1)
                for c in range(IC):
                    if c % 2 == 0:
                        pe.wait_ge(gelu_done, j * IC + (c + 2))
                    for k in range(HC):
                        for w, xT in ((wi_hi, xT_hi), (wi_hi, xT_lo), (wi_lo, xT_hi)):
                            last = nc.tensor.matmul(preact_chunk(c), w[:, e % 2, k, c * P:(c + 1) * P], xT[:, k, :],
                                                    start=(k == 0 and w is wi_hi and xT is xT_hi),
                                                    stop=(k == HC - 1 and w is wi_lo))
                    last.then_inc(preact_ready, 1)

            def second_product(n, e):
                pe.wait_ge(wo_hi_done, e + 1)
                for i in range(PIECES):
                    tile, half = i // 2, i % 2
                    chunks = range(half * PER, (half + 1) * PER)
                    if half == 0:
                        pe.wait_ge(sums_free, n * 2 + tile)

                    def product(part, c, w, **flags):
                        return nc.tensor.matmul(sums(tile), part[:, c, tile * P:(tile + 1) * P], w[:, e % 2, c, :], **flags)

                    pe.wait_ge(h_hi_done, n * PIECES + (i + 1))
                    for c in chunks:
                        product(h_hi, c, wo_hi, start=(c == 0), stop=False)
                    pe.wait_ge(h_lo_done, n * PIECES + (i + 1))
                    for c in chunks:
                        product(h_lo, c, wo_hi, start=False, stop=False)
                    if tile == 0:
                        if e < E - 1:
                            pe.wait_ge(wo_lo_done, 2 * e + half + 1)
                        elif half == 0:
                            pe.wait_ge(last_wo_lo_done, 1)
                        else:
                            pe.wait_ge(wo_lo_done, 2 * e + 1)
                    for c in chunks:
                        product(h_hi, c, wo_lo, start=False, stop=(c == IC - 1)).then_inc(h_used, 1)

            transpose_x(0)
            for _ in range(WARM_UP // 2):
                nc.tensor.matmul(preact[:, 0, 0:P], ident[:, :], ident[:, :], start=True, stop=True)
            last_begin, begin, end = 0, 0, entry(pe, T_END, MAX_BLOCKS)

            def second_product_of_last_expert(n, e):
                if e > 0:
                    with pe.If(last_begin < begin):
                        second_product(n, e - 1)
                    with pe.Else():
                        pe.nop()

            for e in range(E):
                if e > 0:
                    last_begin, begin, end = begin, end, entry(pe, T_END + e, MAX_BLOCKS)
                with pe.If(begin < end):
                    pe.wait_ge(wi_lo_done, e + 1)
                    with pe.Fori(begin, end) as j:
                        first_product(j, e)
                        transpose_x(j + 1)
                        with pe.If(j > begin):
                            second_product(j, e)
                        with pe.Else():
                            second_product_of_last_expert(j, e)
                            pe.nop()
                    pe.nop()
                with pe.Else():
                    second_product_of_last_expert(begin, e)
                    pe.nop()
            last_begin, begin = begin, end
            second_product_of_last_expert(begin, E)


INPUTS = ["x", "itok_B_0_7", "L0_cond_Wi", "L0_cond_bi", "L0_cond_Wo", "L0_cond_bo", "L0_cond_gamma", "L0_cond_beta"]


def kernel(**inputs):
    import numpy as np
    import concourse.bacc as bacc
    from concourse.bass_utils import run_bass_kernel_spmd

    nc = bacc.Bacc("TRN2", target_bir_lowering=False, num_devices=1)
    arrays, args = {}, []
    for name in INPUTS:
        a = np.ascontiguousarray(inputs[name])
        arrays[name + "_dram"] = a
        args.append(nc.dram_tensor(name + "_dram", a.shape, mybir.dt.from_np(a.dtype), kind="ExternalInput").ap())
    y = nc.dram_tensor("y_dram", inputs["x"].shape, FP32, kind="ExternalOutput").ap()
    expert_ffn(nc, *args, y)
    result = run_bass_kernel_spmd(nc, [arrays], core_ids=[0])
    return result.results[0]["y_dram"]
```
